# Optimizing a Trainium2 kernel written in Bass

```python
import numpy as np
import jax
import jax.numpy as jnp

def _softmax(x, axis=-1):
    return jax.nn.softmax(x, axis=axis)

def _gelu(x):
    return jax.nn.gelu(x, approximate=True)

def _silu(x):
    return jax.nn.silu(x)

def _sigmoid(x):
    return jax.nn.sigmoid(x)

def _layernorm(x, axis=-1, eps=1e-05):
    m = jnp.mean(x, axis=axis, keepdims=True)
    v = jnp.var(x, axis=axis, keepdims=True)
    return (x - m) / jnp.sqrt(v + eps)

def _scatter_add(tgt, idx, src, axis=0):
    return tgt.at[idx].add(src)

def _segment_sum(src, seg, n):
    return jax.ops.segment_sum(src, seg, n)
kernel_name = 'mk_rec_standalone_d1_rec_r8_4e0ca1'

def setup_inputs(seed: int=0):
    np.random.seed(seed)
    _w = jnp.asarray

    def _rec_inputs():
        import jax
        import jax.numpy as jnp
        _rk = jax.random.key(seed)
        r_x = jnp.stack([jax.random.randint(jax.random.fold_in(jax.random.fold_in(_rk, 1), 0), (2048,), 72, 99964, jnp.int32), jax.random.randint(jax.random.fold_in(jax.random.fold_in(_rk, 1), 1), (2048,), 78, 99917, jnp.int32), jax.random.randint(jax.random.fold_in(jax.random.fold_in(_rk, 1), 2), (2048,), 131, 99898, jnp.int32), jax.random.randint(jax.random.fold_in(jax.random.fold_in(_rk, 1), 3), (2048,), 78, 99862, jnp.int32), jax.random.randint(jax.random.fold_in(jax.random.fold_in(_rk, 1), 4), (2048,), 17, 99945, jnp.int32), jax.random.randint(jax.random.fold_in(jax.random.fold_in(_rk, 1), 5), (2048,), 152, 99949, jnp.int32), jax.random.randint(jax.random.fold_in(jax.random.fold_in(_rk, 1), 6), (2048,), 81, 99775, jnp.int32), jax.random.randint(jax.random.fold_in(jax.random.fold_in(_rk, 1), 7), (2048,), 79, 99885, jnp.int32), jax.random.randint(jax.random.fold_in(jax.random.fold_in(_rk, 1), 8), (2048,), 71, 99987, jnp.int32), jax.random.randint(jax.random.fold_in(jax.random.fold_in(_rk, 1), 9), (2048,), 29, 99954, jnp.int32), jax.random.randint(jax.random.fold_in(jax.random.fold_in(_rk, 1), 10), (2048,), 28, 99945, jnp.int32), jax.random.randint(jax.random.fold_in(jax.random.fold_in(_rk, 1), 11), (2048,), 55, 99939, jnp.int32), jax.random.randint(jax.random.fold_in(jax.random.fold_in(_rk, 1), 12), (2048,), 18, 99907, jnp.int32), jax.random.randint(jax.random.fold_in(jax.random.fold_in(_rk, 1), 13), (2048,), 3, 99946, jnp.int32), jax.random.randint(jax.random.fold_in(jax.random.fold_in(_rk, 1), 14), (2048,), 6, 99946, jnp.int32), jax.random.randint(jax.random.fold_in(jax.random.fold_in(_rk, 1), 15), (2048,), 190, 99935, jnp.int32), jax.random.randint(jax.random.fold_in(jax.random.fold_in(_rk, 1), 16), (2048,), 96, 99865, jnp.int32), jax.random.randint(jax.random.fold_in(jax.random.fold_in(_rk, 1), 17), (2048,), 20, 99964, jnp.int32), jax.random.randint(jax.random.fold_in(jax.random.fold_in(_rk, 1), 18), (2048,), 45, 99917, jnp.int32), jax.random.randint(jax.random.fold_in(jax.random.fold_in(_rk, 1), 19), (2048,), 32, 99942, jnp.int32), jax.random.randint(jax.random.fold_in(jax.random.fold_in(_rk, 1), 20), (2048,), 1, 99938, jnp.int32), jax.random.randint(jax.random.fold_in(jax.random.fold_in(_rk, 1), 21), (2048,), 5, 99978, jnp.int32), jax.random.randint(jax.random.fold_in(jax.random.fold_in(_rk, 1), 22), (2048,), 1, 12483, jnp.int32), jax.random.randint(jax.random.fold_in(jax.random.fold_in(_rk, 1), 23), (2048,), 131, 99973, jnp.int32), jax.random.randint(jax.random.fold_in(jax.random.fold_in(_rk, 1), 24), (2048,), 46, 99986, jnp.int32), jax.random.randint(jax.random.fold_in(jax.random.fold_in(_rk, 1), 25), (2048,), 11, 12488, jnp.int32), jax.random.randint(jax.random.fold_in(jax.random.fold_in(_rk, 1), 26), (2048,), 22, 99973, jnp.int32), jax.random.randint(jax.random.fold_in(jax.random.fold_in(_rk, 1), 27), (2048,), 33, 99714, jnp.int32), jax.random.randint(jax.random.fold_in(jax.random.fold_in(_rk, 1), 28), (2048,), 39, 99987, jnp.int32), jax.random.randint(jax.random.fold_in(jax.random.fold_in(_rk, 1), 29), (2048,), 97, 99990, jnp.int32), jax.random.randint(jax.random.fold_in(jax.random.fold_in(_rk, 1), 30), (2048,), 15, 99971, jnp.int32), jax.random.randint(jax.random.fold_in(jax.random.fold_in(_rk, 1), 31), (2048,), 14, 99990, jnp.int32)], axis=0)
        return r_x
    r_x = _rec_inputs()

    def _L0_rec_setup():
        import jax, jax.numpy as jnp
        import numpy as np
        F = 32
        B = 256
        K = 64
        H = 64
        VOCAB = 12500
        key = jax.random.key(seed)
        ks = jax.random.split(key, 7)
        x = jax.random.randint(ks[0], (F, B), 0, VOCAB)
        emb_v = jax.random.normal(ks[1], (VOCAB, K), jnp.float32) * 0.05
        at_w = jax.random.normal(ks[2], (K, H), jnp.float32) * 0.1
        at_b = jnp.zeros((H,), jnp.float32)
        at_h = jax.random.normal(ks[3], (H, 1), jnp.float32) * 0.1
        p = jax.random.normal(ks[4], (K, 1), jnp.float32) * 0.1
        w0 = jnp.zeros((), jnp.float32)
        w1 = jax.random.normal(ks[5], (VOCAB, 1), jnp.float32) * 0.05
        return {'x': x, 'emb_v': emb_v, 'at_w': at_w, 'at_b': at_b, 'at_h': at_h, 'p': p, 'w0': w0, 'w1': w1}
    _L0_rec_all = _L0_rec_setup()
    _L0_rec_in = {k: v for k, v in _L0_rec_all.items() if k in ('emb_v', 'at_w', 'at_b', 'at_h', 'p', 'w0', 'w1')}
    del _L0_rec_all
    return {'r_x': r_x, 'L0_rec_emb_v': _L0_rec_in['emb_v'], 'L0_rec_at_w': _L0_rec_in['at_w'], 'L0_rec_at_b': _L0_rec_in['at_b'], 'L0_rec_at_h': _L0_rec_in['at_h'], 'L0_rec_p': _L0_rec_in['p'], 'L0_rec_w0': _L0_rec_in['w0'], 'L0_rec_w1': _L0_rec_in['w1']}

def reference(r_x, L0_rec_emb_v, L0_rec_at_w, L0_rec_at_b, L0_rec_at_h, L0_rec_p, L0_rec_w0, L0_rec_w1):
    import jax
    import jax.numpy as jnp

    def _L0_rec_ref(x, emb_v, at_w, at_b, at_h, p, w0, w1):
        import jax, jax.numpy as jnp
        import numpy as np
        F = 32
        B = 256
        K = 64
        H = 64
        VOCAB = 12500
        V = emb_v[x]
        iu, ju = np.triu_indices(F, k=1)
        VV = V[iu] * V[ju]
        hid = jax.nn.relu(jnp.einsum('pbk,kh->pbh', VV, at_w) + at_b)
        score = jnp.einsum('pbh,ho->pbo', hid, at_h)
        pooled = jnp.sum(VV * score, axis=0)
        at_fm_score = pooled @ p
        fm1 = w0 + jnp.sum(w1[x], axis=0)
        logit = at_fm_score + fm1
        prob = jax.nn.sigmoid(logit)
        return prob
    y = _L0_rec_ref(r_x, L0_rec_emb_v, L0_rec_at_w, L0_rec_at_b, L0_rec_at_h, L0_rec_p, L0_rec_w0, L0_rec_w1)
    return y

_drawn_inputs = setup_inputs


def setup_inputs(seed=0):
    import zlib

    import numpy as np

    out = dict(_drawn_inputs(seed))
    spreads = {'L0_rec_at_b': (0.0, 0.8)}
    factors = {'L0_rec_emb_v': 5.784,
     'L0_rec_at_w': 8.0,
     'L0_rec_at_h': 8.0,
     'L0_rec_p': 7.795,
     'L0_rec_w1': 7.883}
    for name, (base, spread) in spreads.items():
        noise = np.random.default_rng([zlib.crc32(name.encode()), seed]).standard_normal(out[name].shape)
        drawn = base * np.exp(spread * noise) if base else spread * noise
        out[name] = jnp.asarray(drawn.astype(out[name].dtype))
    for name, factor in factors.items():
        out[name] = (out[name] * factor).astype(out[name].dtype)
    return out
```

```python
from contextlib import ExitStack

import concourse.bass as bass
from concourse import mybir

FIELDS, BATCH, EMB, HID, VOCAB = 32, 2048, 64, 64, 12500
QUARTERS = 4
NB = BATCH // QUARTERS
NM = NB // QUARTERS
FILL_M = 4
FILLS = NM // FILL_M
GROUP = FILL_M * QUARTERS
TILES = 2 * FILL_M
GATHERS = 2 * TILES
STEPS = FIELDS // 4
ROUNDS = 2 * STEPS
COLS = GROUP * FIELDS
X_SLOTS, Z_SLOTS, H_SLOTS = 8, 2, 4
ROW = EMB + 1
EMB_AT, W1_AT = (1, 0), (0, EMB)
TAB_ROWS = VOCAB // 128
TAB_TAIL = VOCAB - 128 * TAB_ROWS


def segments(s):
    n = FIELDS - 1 - 2 * s
    return [(s, FIELDS - n, n, 0), (STEPS * 2 - 1 - s, n, FIELDS - n, GROUP * n)]


def afm_kernel(nc, r_x, emb_v, at_w, at_b, at_h, p, w0, w1, out):
    fp32, bf16 = mybir.dt.float32, mybir.dt.bfloat16
    int32, uint32 = mybir.dt.int32, mybir.dt.uint32
    ALU = mybir.AluOpType
    ACT = mybir.ActivationFunctionType
    AX = mybir.AxisListType

    table = [nc.dram_tensor(f"table{half}", (VOCAB, ROW), fp32, kind="Internal").ap() for half in range(2)]

    ctx = ExitStack()
    with ctx:
        def sb(name, shape, dt=fp32):
            return ctx.enter_context(nc.sbuf_tensor(name, shape, dt))

        def ps(name, shape):
            return ctx.enter_context(nc.psum_tensor(name, shape, fp32))

        def sem(name):
            return ctx.enter_context(nc.semaphore(name))

        w_sb = sb("w_sb", [128, HID])
        bias = sb("bias", [128, 1])
        hcol = sb("hcol", [128, 1])
        pcol = sb("pcol", [128, 1])
        w0_sb = sb("w0_sb", [QUARTERS, 1])
        ident = sb("ident", [128, 128])
        score_w = sb("score_w", [128, FIELDS // 2, FIELDS])
        zeros = sb("zeros", [128, COLS], bf16)
        upper = sb("upper", [128, FIELDS])
        jrow_i = sb("jrow_i", [128, FIELDS], int32)
        prow_i = sb("prow_i", [128, 1], int32)
        imod = sb("imod", [128, 1], int32)
        irow = sb("irow", [128, 1])
        pick = sb("pick", [128, QUARTERS, 2 * QUARTERS - 1])
        idx_raw = sb("idx_raw", [128, NB], int32)
        idx_wrap = sb("idx_wrap", [128, NB])
        idx_sum = sb("idx_sum", [128, NB])
        idx = sb("idx", [128, NB], uint32)
        idx_stage = [sb(f"idx_stage{i}", [128, QUARTERS, FILL_M], uint32) for i in range(2)]
        raw = sb("raw", [128, TAB_ROWS, EMB])
        raw_w1 = sb("raw_w1", [128, TAB_ROWS])
        joined = [sb(f"joined{half}", [128, TAB_ROWS + 1, ROW]) for half in range(2)]
        rows = [sb(f"rows{i}", [128, TILES, 2, ROW]) for i in range(2)]
        V = [sb(f"V{i}", [128, 2, GROUP, FIELDS]) for i in range(2)]
        pV = [sb(f"pV{i}", [128, 2, GROUP, FIELDS]) for i in range(2)]
        X = sb("X", [128, X_SLOTS, 2, COLS])
        H = sb("H", [128, H_SLOTS, 2, COLS])
        gram = sb("gram", [128, GROUP, FIELDS])
        prod = sb("prod", [128, GROUP, FIELDS])
        part = sb("part", [128, FILLS * GROUP])
        w1_all = sb("w1_all", [128, QUARTERS, NM])
        y_sb = sb("y_sb", [QUARTERS, NB])

        Z = ps("Z", [128, Z_SLOTS, 2, COLS])
        S = ps("S", [128, GROUP, FIELDS])
        G = ps("G", [128, GROUP, FIELDS])
        TR = ps("TR", [128, 2, COLS])

        idx_loaded = sem("idx_loaded")
        idx_chain = sem("idx_chain")
        idx_ready = sem("idx_ready")
        idx_staged = sem("idx_staged")
        raw_loaded = sem("raw_loaded")
        tail_loaded = sem("tail_loaded")
        rows_joined = sem("rows_joined")
        table_stored = sem("table_stored")
        small_loaded = sem("small_loaded")
        iotas_ready = sem("iotas_ready")
        mask_chain = sem("mask_chain")
        consts_ready = sem("consts_ready")
        score_w_cleared = sem("score_w_cleared")
        ident_cleared = sem("ident_cleared")
        ident_ready = sem("ident_ready")
        w1_first = sem("w1_first")
        rows_gathered = [sem(f"rows_gathered{i}") for i in range(2)]
        rows_turned = sem("rows_turned")
        w1_kept = sem("w1_kept")
        v_ready = sem("v_ready")
        pv_ready = sem("pv_ready")
        x_ready = sem("x_ready")
        z_ready = sem("z_ready")
        hid_ready = sem("hid_ready")
        scored = sem("scored")
        gram_ready = sem("gram_ready")
        gram_masked = sem("gram_masked")
        prod_ready = sem("prod_ready")
        part_ready = sem("part_ready")
        logit_ready = sem("logit_ready")
        y_ready = sem("y_ready")
        y_stored = sem("y_stored")

        block = ctx.enter_context(nc.Block())

        def over_fills(eng, fill):
            fill(0, 0, True, False)
            with eng.Fori(1, FILLS - 2, 2) as t:
                fill(t, 1, False, False)
                fill(t + 1, 0, False, False)
            fill(FILLS - 1, (FILLS - 1) % 2, False, True)

        def gathered(t, parity):
            return 16 * GATHERS // 2 * (t - parity) + 16 * GATHERS

        @block.sync
        def _(sp):
            for q in range(QUARTERS):
                sp.dma_start(idx_raw[q * FIELDS:(q + 1) * FIELDS, :],
                             r_x[:, q * NB:(q + 1) * NB]).then_inc(idx_loaded, 16)
            for half in range(2):
                lo, hi = half * 64, half * 64 + 64
                sp.dma_start(pcol[lo:hi, :], p).then_inc(small_loaded, 16)
                sp.dma_start(w_sb[lo:hi, :], at_w).then_inc(small_loaded, 16)
                sp.dma_start(bias[lo:hi, :], at_b.rearrange("(h o) -> h o", o=1)).then_inc(small_loaded, 16)
                sp.dma_start(hcol[lo:hi, :], at_h).then_inc(small_loaded, 16)
            sp.dma_start(w0_sb[:, :], w0.to_broadcast([QUARTERS, 1])).then_inc(small_loaded, 16)
            main = 128 * TAB_ROWS
            sp.dma_start(raw[:, :, :], emb_v[0:main, :].rearrange("(p r) k -> p r k", p=128)).then_inc(raw_loaded, 16)
            sp.dma_start(raw_w1[:, :], w1[0:main, :].rearrange("(p r) o -> p (r o)", p=128)).then_inc(raw_loaded, 16)
            for half in range(2):
                tail = joined[half][0:TAB_TAIL, TAB_ROWS, :]
                sp.dma_start(tail[:, EMB_AT[half]:EMB_AT[half] + EMB], emb_v[main:VOCAB, :]).then_inc(tail_loaded, 16)
                sp.dma_start(tail[:, W1_AT[half]:W1_AT[half] + 1], w1[main:VOCAB, :]).then_inc(tail_loaded, 16)
            sp.wait_ge(tail_loaded, 64)
            for half in range(2):
                sp.wait_ge(rows_joined, 2 * half + 2)
                sp.dma_start(table[half][0:main, :].rearrange("(p r) k -> p r k", p=128),
                             joined[half][:, 0:TAB_ROWS, :]).then_inc(table_stored, 16)
                sp.dma_start(table[half][main:VOCAB, :], joined[half][0:TAB_TAIL, TAB_ROWS, :]).then_inc(table_stored, 16)
            sp.wait_ge(y_ready, 1)
            sp.dma_start(out.rearrange("(q n) o -> q (n o)", q=QUARTERS), y_sb[:, :]).then_inc(y_stored, 16)
            sp.wait_ge(y_stored, 16)

        @block.gpsimd
        def _(pool):
            nc.gpsimd.iota(prow_i[:, :], pattern=[[0, 1]], base=0, channel_multiplier=1)
            nc.gpsimd.iota(jrow_i[:, :], pattern=[[1, FIELDS]], base=0, channel_multiplier=0).then_inc(iotas_ready, 1)
            nc.gpsimd.memset(ident[:, :], 0.0).then_inc(ident_cleared, 1)
            pool.wait_ge(ident_cleared, 1)
            nc.gpsimd.affine_select(out=ident[:, :], in_=ident[:, :], compare_op=ALU.not_equal, fill=1.0, base=0,
                                    pattern=[[-1, 128]], channel_multiplier=1).then_inc(ident_ready, 1)

            def gather(t, parity, first):
                stage = idx_stage[parity]
                nc.gpsimd.tensor_copy(stage[:, :, :],
                                      idx[:, :].rearrange("p (a m) -> p a m", a=QUARTERS)[:, :, bass.ds(t * FILL_M, FILL_M)]
                                      ).then_inc(idx_staged, 1)
                pool.wait_ge(idx_staged, t + 1)
                pool.nop(nofuse=True)
                for g in range(2):
                    for m in range(FILL_M):
                        for half in range(2):
                            at = bass.IndirectOffsetOnAxis(ap=stage[:, 2 * half + g, m:m + 1], axis=0)
                            c0, c1 = (EMB_AT[half], EMB_AT[half] + EMB) if first else (0, ROW)
                            pool.indirect_dma_start(out=rows[parity][:, g * FILL_M + m, half, c0:c1],
                                                    out_offset=None, in_=emb_v if first else table[half],
                                                    in_offset=at).then_inc(rows_gathered[parity], 16)

            pool.wait_ge(idx_ready, 1)
            gather(0, 0, True)
            for g in range(2):
                for m in range(FILL_M):
                    for half in range(2):
                        at = bass.IndirectOffsetOnAxis(ap=idx_stage[0][:, 2 * half + g, m:m + 1], axis=0)
                        pool.indirect_dma_start(out=rows[0][:, g * FILL_M + m, half, W1_AT[half]:W1_AT[half] + 1], out_offset=None,
                                                in_=w1, in_offset=at).then_inc(w1_first, 16)
            pool.wait_ge(table_stored, 64)
            gather(1, 1, False)

            def refill(t, parity):
                pool.wait_ge(rows_turned, 2 * (t - 1))
                pool.wait_ge(w1_kept, 2 * (t - 1))
                gather(t, parity, False)

            with pool.Fori(2, FILLS - 1, 2) as t:
                refill(t, 0)
                refill(t + 1, 1)

        @block.vector
        def _(dve):
            dve.wait_ge(idx_loaded, 16 * QUARTERS)
            nc.vector.tensor_scalar(idx_wrap[:, :], idx_raw[:, :], 0.0, float(VOCAB), ALU.is_lt, ALU.mult).then_inc(idx_chain, 1)
            dve.wait_ge(idx_chain, 1)
            nc.vector.tensor_tensor(idx_sum[:, :], idx_raw[:, :], idx_wrap[:, :], ALU.add).then_inc(idx_chain, 1)
            dve.wait_ge(idx_chain, 2)
            nc.vector.tensor_scalar(idx[:, :], idx_sum[:, :], 0.0, float(VOCAB - 1), ALU.max, ALU.min).then_inc(idx_ready, 1)

            nc.vector.memset(zeros[:, :], 0.0)
            nc.vector.memset(score_w[:, :, :], 0.0).then_inc(score_w_cleared, 1)
            nc.vector.memset(pick[:, :, :], 0.0).then_inc(mask_chain, 1)
            dve.wait_ge(iotas_ready, 1)
            dve.wait_ge(mask_chain, 1)
            for Q in range(QUARTERS):
                nc.vector.memset(pick[32 * Q:32 * Q + 32, Q, QUARTERS - 1:QUARTERS], 1.0)
            nc.vector.tensor_scalar(imod[:, :], prow_i[:, :], FIELDS - 1, None, ALU.bitwise_and).then_inc(mask_chain, 1)
            dve.wait_ge(mask_chain, 2)
            nc.vector.tensor_copy(irow[:, :], imod[:, :]).then_inc(mask_chain, 1)
            dve.wait_ge(mask_chain, 3)
            nc.vector.tensor_scalar(upper[:, :], jrow_i[:, :], irow[:, :], None, ALU.is_gt).then_inc(mask_chain, 1)
            dve.wait_ge(small_loaded, 16 * 9)
            dve.wait_ge(score_w_cleared, 1)
            for par in range(2):
                rng = slice(64 * par, 64 * par + 64)
                for slot in range(FIELDS // 2):
                    last = nc.vector.tensor_copy(score_w[rng, slot, 2 * slot + par:2 * slot + par + 1], hcol[rng, :])
            last.then_inc(consts_ready, 1)
            dve.wait_ge(mask_chain, 4)

            def pair_sums(t, r):
                if r == 2:
                    dve.wait_ge(gram_ready, t + 1)
                    nc.vector.tensor_tensor(gram[:, :, :], G[:, :, :],
                                            upper[:, :].unsqueeze(1).to_broadcast([128, GROUP, FIELDS]),
                                            ALU.mult).then_inc(gram_masked, 1)
                if r == 3:
                    dve.wait_ge(gram_masked, t + 1)
                    dve.wait_ge(scored, STEPS * (t + 1))
                    nc.vector.tensor_tensor(prod[:, :, :], S[:, :, :], gram[:, :, :], ALU.mult).then_inc(prod_ready, 1)
                if r == 4:
                    dve.wait_ge(prod_ready, t + 1)
                    nc.vector.tensor_reduce(part[:, bass.ds(t * GROUP, GROUP)], prod[:, :, :], AX.X, ALU.add
                                            ).then_inc(part_ready, 1)

            def products(t, parity, first, last):
                for s in range(STEPS):
                    for g in range(2):
                        r = 2 * s + g
                        n = ROUNDS * t + r
                        if s == 0:
                            dve.wait_ge(v_ready, 2 * t + g + 1)
                        if not first or r >= X_SLOTS:
                            dve.wait_ge(z_ready, n + 1 - X_SLOTS)
                        for slot, j0, nj, c0 in segments(s):
                            shape = [128, 2, GROUP, nj]
                            vj = V[parity][:, g, :, j0:FIELDS].unsqueeze(1).to_broadcast(shape)
                            vi = V[parity][:, g, :, 2 * slot:2 * slot + 2].rearrange("p b c -> p c b").unsqueeze(3).to_broadcast(shape)
                            xo = X[:, r % X_SLOTS, :, c0:c0 + GROUP * nj].rearrange("p c (b j) -> p c b j", j=nj)
                            last_one = nc.vector.tensor_tensor(xo, vj, vi, ALU.mult)
                        last_one.then_inc(x_ready, 1)
                        if not first:
                            pair_sums(t - 1, r)

            over_fills(dve, products)
            for r in (2, 3, 4):
                pair_sums(FILLS - 1, r)

        @block.scalar
        def _(act):
            act.wait_ge(raw_loaded, 32)
            for half in range(2):
                nc.scalar.copy(joined[half][:, 0:TAB_ROWS, W1_AT[half]], raw_w1[:, :]).then_inc(rows_joined, 1)
                nc.scalar.copy(joined[half][:, 0:TAB_ROWS, EMB_AT[half]:EMB_AT[half] + EMB], raw[:, :, :]
                               ).then_inc(rows_joined, 1)

            def evacuate(t, parity, first, k):
                if k < 2:
                    act.wait_ge(rows_turned, 2 * t + k + 1)
                    if k == 0 and not first:
                        act.wait_ge(x_ready, ROUNDS * (t - 1))
                        act.wait_ge(gram_ready, t - 1)
                    nc.scalar.copy(V[parity][:, k, :, :], TR[:, k, :].rearrange("p (b f) -> p b f", f=FIELDS)
                                   ).then_inc(v_ready, 1)
                elif k < 4:
                    nc.scalar.activation(pV[parity][:, k - 2, :, :],
                                         TR[:, k - 2, :].rearrange("p (b f) -> p b f", f=FIELDS),
                                         ACT.Copy, scale=pcol[:, 0:1]).then_inc(pv_ready, 1)
                else:
                    w1s = rows[parity][:, :, :, :].rearrange("p t h k -> p t (h k)")
                    for half in range(2):
                        src = w1s[:, :, half * (2 * ROW - 1)].rearrange("p (g m) -> p g m", g=2)
                        nc.scalar.copy(w1_all[:, 2 * half:2 * half + 2, bass.ds(t * FILL_M, FILL_M)], src
                                       ).then_inc(w1_kept, 1)

            act.wait_ge(small_loaded, 16 * 9)
            for k in range(4):
                evacuate(0, 0, True, k)
            act.wait_ge(w1_first, 16 * GATHERS)
            evacuate(0, 0, True, 4)

            def relus(t, parity, first, last):
                for r in range(ROUNDS):
                    n = ROUNDS * t + r
                    act.wait_ge(z_ready, n + 1)
                    if not first or r >= H_SLOTS:
                        act.wait_ge(scored, STEPS * t + r // 2 - 1)
                    nc.scalar.activation(H[:, r % H_SLOTS, :, :], Z[:, r % Z_SLOTS, :, :], ACT.Relu,
                                         bias=bias[:, 0:1]).then_inc(hid_ready, 1)
                    if r >= 9 and r < 14 and not last:
                        evacuate(t + 1, 1 - parity, first, r - 9)

            over_fills(act, relus)
            act.wait_ge(logit_ready, 1)
            nc.scalar.activation(y_sb[:, :], TR[0:QUARTERS, 0, :], ACT.Sigmoid, bias=w0_sb[:, 0:1]).then_inc(y_ready, 1)

        @block.tensor
        def _(pe):
            def turn(t, parity):
                pe.wait_ge(rows_gathered[parity], gathered(t, parity))
                embs = rows[parity][:, :, :, :].rearrange("p t h k -> p t (h k)")
                for g in range(2):
                    for m in range(FILL_M):
                        last = nc.tensor.transpose(TR[:, g, 128 * m:128 * m + 128],
                                                   embs[:, g * FILL_M + m, 1:1 + 2 * EMB], ident[:, :])
                    last.then_inc(rows_turned, 1)

            def hidden(t, r, first):
                n = ROUNDS * t + r
                pe.wait_ge(x_ready, n + 1)
                if not first or r >= Z_SLOTS:
                    pe.wait_ge(hid_ready, n + 1 - Z_SLOTS)
                pe.nop(nofuse=True)
                for half, par in ((0, 0), (1, 1), (0, 1), (1, 0)):
                    k, c = 64 * half, 64 * par
                    last = nc.tensor.matmul(Z[c:c + 64, r % Z_SLOTS, half, :], w_sb[k:k + 64, :],
                                            X[k:k + 64, r % X_SLOTS, par, :], start=True, stop=True)
                last.then_inc(z_ready, 1)

            def clear_scores(t, first):
                if not first:
                    pe.wait_ge(prod_ready, t)
                for Q in range(QUARTERS):
                    nc.tensor.matmul(S[32 * Q:32 * Q + 32, :, :], zeros[:, 0:32],
                                     zeros[:, :].rearrange("p (b j) -> p b j", j=FIELDS), start=True, stop=False)

            def scores(t, s):
                pe.wait_ge(hid_ready, ROUNDS * t + 2 * s + 2)
                for k, (slot, j0, nj, c0) in enumerate(segments(s)):
                    for g in range(2):
                        for half in range(2):
                            Q = 2 * half + g
                            hid = H[:, (2 * s + g) % H_SLOTS, half, c0:c0 + GROUP * nj]
                            last = nc.tensor.matmul(S[32 * Q:32 * Q + 32, :, j0:FIELDS],
                                                    score_w[:, slot, :],
                                                    hid.rearrange("p (b j) -> p b j", j=nj),
                                                    start=False, stop=(s == STEPS - 1 and k == 1))
                last.then_inc(scored, 1)

            def grams(t, parity, first):
                pe.wait_ge(pv_ready, 2 * t + 2)
                if not first:
                    pe.wait_ge(gram_masked, t)
                pe.nop(nofuse=True)
                for b in range(GROUP):
                    for Q in range(QUARTERS):
                        half, g = divmod(Q, 2)
                        k = slice(64 * half, 64 * half + 64)
                        last = nc.tensor.matmul(G[32 * Q:32 * Q + 32, b, :],
                                                V[parity][k, g, b, :],
                                                pV[parity][k, g, b, :], start=(b == 0), stop=(b == GROUP - 1),
                                                skip_group_check=True)
                last.then_inc(gram_ready, 1)

            pe.wait_ge(ident_ready, 1)
            pe.wait_ge(consts_ready, 1)
            turn(0, 0)

            def products(t, parity, first, last):
                for s in range(STEPS):
                    hidden(t, 2 * s, first)
                    hidden(t, 2 * s + 1, first)
                    if s == 1:
                        clear_scores(t, first)
                    if s > 0:
                        scores(t, s - 1)
                    if s == 3 and not last:
                        pe.wait_ge(pv_ready, 2 * t + 2)
                        turn(t + 1, 1 - parity)
                grams(t, parity, first)
                scores(t, STEPS - 1)

            over_fills(pe, products)

            pe.wait_ge(w1_kept, 2 * FILLS)
            pe.wait_ge(part_ready, FILLS)
            logit = TR[0:QUARTERS, 0, :]
            nc.tensor.matmul(logit, pick[:, :, QUARTERS - 1], w1_all[:, :, :].rearrange("p a m -> p (a m)"),
                             start=True, stop=False)
            by_q = part[:, :].rearrange("p (m q) -> p q m", q=QUARTERS)
            for Q in range(QUARTERS):
                for q in range(QUARTERS):
                    last = nc.tensor.matmul(logit[:, Q * NM:(Q + 1) * NM],
                                            pick[:, Q, QUARTERS - 1 - q:2 * QUARTERS - 1 - q], by_q[:, q, :],
                                            start=False, stop=(Q == QUARTERS - 1 and q == QUARTERS - 1))
            last.then_inc(logit_ready, 1)


_INS = ["r_x", "L0_rec_emb_v", "L0_rec_at_w", "L0_rec_at_b", "L0_rec_at_h", "L0_rec_p", "L0_rec_w0", "L0_rec_w1"]


def kernel(**inputs):
    import numpy as _np
    import concourse.bacc as _bacc
    from concourse import mybir as _mybir
    from concourse.bass_utils import run_bass_kernel_spmd as _run

    nc = _bacc.Bacc("TRN2", target_bir_lowering=False, num_devices=1)
    arrays, args = {}, []
    for name in _INS:
        a = _np.ascontiguousarray(inputs[name])
        if a.ndim == 0:
            a = a.reshape(1, 1)
        arrays[f"in_{name}_dram"] = a
        args.append(nc.dram_tensor(f"in_{name}_dram", a.shape, _mybir.dt.from_np(a.dtype), kind="ExternalInput").ap())
    out = nc.dram_tensor("out_dram", (BATCH, 1), _mybir.dt.float32, kind="ExternalOutput").ap()
    afm_kernel(nc, *args, out)
    r = _run(nc, [arrays], core_ids=[0])
    return r.results[0]["out_dram"]
```

```python
from contextlib import ExitStack

import concourse.bass as bass
from concourse import mybir

FIELDS, BATCH, EMB, HID, VOCAB = 32, 2048, 64, 64, 12500
QUARTERS = 4
NB = BATCH // QUARTERS
NM = NB // QUARTERS
FILL_M = 4
FILLS = NM // FILL_M
GROUP = FILL_M * QUARTERS
TILES = 2 * FILL_M
GATHERS = 2 * TILES
STEPS = FIELDS // 4
ROUNDS = 2 * STEPS
COLS = GROUP * FIELDS
ORDER = [(s, g) for four in (0, 4) for g in range(2) for s in range(four, four + 4)]
SCORED_AFTER = {6: (0, 1), 8: (2, 3), 14: (4, 5)}
LAST_STEPS, LAST_AFTER = (6, 7), 1
GRAMS_AFTER = (4, 6, 10, 14)
BATCHES = 4
X_SLOTS, Z_SLOTS, H_SLOTS = 8, 2, 8
ROW = EMB + 1
EMB_AT, W1_AT = (1, 0), (0, EMB)
TAB_ROWS = VOCAB // 128
TAB_TAIL = VOCAB - 128 * TAB_ROWS


def segments(s):
    n = FIELDS - 1 - 2 * s
    return [(s, FIELDS - n, n, 0), (STEPS * 2 - 1 - s, n, FIELDS - n, GROUP * n)]


def afm_kernel(nc, r_x, emb_v, at_w, at_b, at_h, p, w0, w1, out):
    fp32, bf16 = mybir.dt.float32, mybir.dt.bfloat16
    int32, uint32 = mybir.dt.int32, mybir.dt.uint32
    ALU = mybir.AluOpType
    ACT = mybir.ActivationFunctionType
    AX = mybir.AxisListType

    table = [nc.dram_tensor(f"table{half}", (VOCAB, ROW), fp32, kind="Internal").ap() for half in range(2)]

    ctx = ExitStack()
    with ctx:
        def sb(name, shape, dt=fp32):
            return ctx.enter_context(nc.sbuf_tensor(name, shape, dt))

        def ps(name, shape):
            return ctx.enter_context(nc.psum_tensor(name, shape, fp32))

        def sem(name):
            return ctx.enter_context(nc.semaphore(name))

        w_sb = sb("w_sb", [128, HID])
        bias = sb("bias", [128, 1])
        hcol = sb("hcol", [128, 1])
        pcol = sb("pcol", [128, 1])
        w0_sb = sb("w0_sb", [QUARTERS, 1])
        ident = sb("ident", [128, 128])
        score_w = sb("score_w", [128, FIELDS // 2, FIELDS])
        zeros = sb("zeros", [128, COLS], bf16)
        upper = sb("upper", [128, FIELDS])
        jrow_i = sb("jrow_i", [128, FIELDS], int32)
        prow_i = sb("prow_i", [128, 1], int32)
        imod = sb("imod", [128, 1], int32)
        irow = sb("irow", [128, 1])
        pick = sb("pick", [128, QUARTERS, 2 * QUARTERS - 1])
        idx_raw = sb("idx_raw", [128, NB], int32)
        idx_wrap = sb("idx_wrap", [128, NB])
        idx_sum = sb("idx_sum", [128, NB])
        idx = sb("idx", [128, NB], uint32)
        idx_stage = [sb(f"idx_stage{i}", [128, QUARTERS, FILL_M], uint32) for i in range(2)]
        raw = sb("raw", [128, TAB_ROWS, EMB])
        raw_w1 = sb("raw_w1", [128, TAB_ROWS])
        joined = [sb(f"joined{half}", [128, TAB_ROWS + 1, ROW]) for half in range(2)]
        rows = [sb(f"rows{i}", [128, TILES, 2, ROW]) for i in range(2)]
        V = [sb(f"V{i}", [128, 2, GROUP, FIELDS]) for i in range(2)]
        pV = [sb(f"pV{i}", [128, 2, GROUP, FIELDS]) for i in range(2)]
        X = sb("X", [128, X_SLOTS, 2, COLS])
        H = sb("H", [128, H_SLOTS, 2, COLS])
        gram = sb("gram", [128, GROUP, FIELDS])
        prod = sb("prod", [128, GROUP, FIELDS])
        part = sb("part", [128, FILLS * GROUP])
        w1_all = sb("w1_all", [128, QUARTERS, NM])
        y_sb = sb("y_sb", [QUARTERS, QUARTERS, NM])
        warm = sb("warm", [QUARTERS, 1])

        Z = ps("Z", [128, Z_SLOTS, 2, COLS])
        S = ps("S", [128, GROUP, FIELDS])
        G = ps("G", [128, GROUP, FIELDS])
        TR = ps("TR", [128, 2, COLS])
        logit = TR[0:QUARTERS, 0, :]

        idx_loaded = sem("idx_loaded")
        idx_chain = sem("idx_chain")
        idx_ready = sem("idx_ready")
        idx_staged = sem("idx_staged")
        raw_loaded = sem("raw_loaded")
        tail_loaded = sem("tail_loaded")
        rows_joined = sem("rows_joined")
        table_stored = sem("table_stored")
        small_loaded = sem("small_loaded")
        iotas_ready = sem("iotas_ready")
        mask_chain = sem("mask_chain")
        consts_ready = sem("consts_ready")
        score_w_cleared = sem("score_w_cleared")
        ident_cleared = sem("ident_cleared")
        ident_ready = sem("ident_ready")
        w1_first = sem("w1_first")
        first_rows = [sem(f"first_rows{g}") for g in range(2)]
        second_rows = sem("second_rows")
        rows_gathered = [sem(f"rows_gathered{i}") for i in range(2)]
        rows_turned = sem("rows_turned")
        w1_kept = sem("w1_kept")
        v_ready = sem("v_ready")
        pv_ready = sem("pv_ready")
        x_ready = sem("x_ready")
        z_ready = sem("z_ready")
        hid_ready = sem("hid_ready")
        scored = sem("scored")
        gram_ready = sem("gram_ready")
        gram_masked = sem("gram_masked")
        prod_ready = sem("prod_ready")
        part_ready = sem("part_ready")
        sigmoid_loaded = sem("sigmoid_loaded")
        logit_ready = sem("logit_ready")
        y_ready = sem("y_ready")
        y_stored = sem("y_stored")

        block = ctx.enter_context(nc.Block())

        def over_fills(eng, fill):
            fill(0, 0, True, False)
            with eng.Fori(1, FILLS - 2, 2) as t:
                fill(t, 1, False, False)
                fill(t + 1, 0, False, False)
            fill(FILLS - 1, (FILLS - 1) % 2, False, True)

        def gathered(t, parity):
            return 16 * GATHERS // 2 * (t - parity)

        @block.sync
        def _(sp):
            for q in range(QUARTERS):
                sp.dma_start(idx_raw[q * FIELDS:(q + 1) * FIELDS, :],
                             r_x[:, q * NB:(q + 1) * NB]).then_inc(idx_loaded, 16)
            for half in range(2):
                lo, hi = half * 64, half * 64 + 64
                sp.dma_start(pcol[lo:hi, :], p).then_inc(small_loaded, 16)
                sp.dma_start(w_sb[lo:hi, :], at_w).then_inc(small_loaded, 16)
                sp.dma_start(bias[lo:hi, :], at_b.rearrange("(h o) -> h o", o=1)).then_inc(small_loaded, 16)
                sp.dma_start(hcol[lo:hi, :], at_h).then_inc(small_loaded, 16)
            sp.dma_start(w0_sb[:, :], w0.to_broadcast([QUARTERS, 1])).then_inc(small_loaded, 16)
            sp.wait_ge(first_rows[1], 16 * GATHERS // 2)
            main = 128 * TAB_ROWS
            sp.dma_start(raw[:, :, :], emb_v[0:main, :].rearrange("(p r) k -> p r k", p=128)).then_inc(raw_loaded, 16)
            sp.dma_start(raw_w1[:, :], w1[0:main, :].rearrange("(p r) o -> p (r o)", p=128)).then_inc(raw_loaded, 16)
            for half in range(2):
                tail = joined[half][0:TAB_TAIL, TAB_ROWS, :]
                sp.dma_start(tail[:, EMB_AT[half]:EMB_AT[half] + EMB], emb_v[main:VOCAB, :]).then_inc(tail_loaded, 16)
                sp.dma_start(tail[:, W1_AT[half]:W1_AT[half] + 1], w1[main:VOCAB, :]).then_inc(tail_loaded, 16)
            sp.wait_ge(tail_loaded, 64)
            for half in range(2):
                sp.wait_ge(rows_joined, 6 * half + 6)
                sp.dma_start(table[half][0:main, :].rearrange("(p r) k -> p r k", p=128),
                             joined[half][:, 0:TAB_ROWS, :]).then_inc(table_stored, 16)
                sp.dma_start(table[half][main:VOCAB, :], joined[half][0:TAB_TAIL, TAB_ROWS, :]).then_inc(table_stored, 16)
            sp.wait_ge(y_ready, 1)
            sp.dma_start(out.rearrange("(q a m) o -> a q (m o)", q=QUARTERS, a=QUARTERS), y_sb[:, :, :]).then_inc(y_stored, 16)
            sp.wait_ge(y_stored, 16)

        @block.gpsimd
        def _(pool):
            nc.gpsimd.iota(prow_i[:, :], pattern=[[0, 1]], base=0, channel_multiplier=1)
            nc.gpsimd.iota(jrow_i[:, :], pattern=[[1, FIELDS]], base=0, channel_multiplier=0).then_inc(iotas_ready, 1)
            nc.gpsimd.memset(ident[:, :], 0.0).then_inc(ident_cleared, 1)
            pool.wait_ge(ident_cleared, 1)
            nc.gpsimd.affine_select(out=ident[:, :], in_=ident[:, :], compare_op=ALU.not_equal, fill=1.0, base=0,
                                    pattern=[[-1, 128]], channel_multiplier=1).then_inc(ident_ready, 1)

            def gather(t, parity, source):
                stage = idx_stage[parity]
                nc.gpsimd.tensor_copy(stage[:, :, :],
                                      idx[:, :].rearrange("p (a m) -> p a m", a=QUARTERS)[:, :, bass.ds(t * FILL_M, FILL_M)]
                                      ).then_inc(idx_staged, 1)
                pool.wait_ge(idx_staged, t + 1)
                pool.nop(nofuse=True)
                for g in range(2):
                    for m in range(FILL_M):
                        for half in range(2):
                            at = bass.IndirectOffsetOnAxis(ap=stage[:, 2 * half + g, m:m + 1], axis=0)
                            joint = source is table
                            c0, c1 = (0, ROW) if joint else (EMB_AT[half], EMB_AT[half] + EMB)
                            arrived = rows_gathered[parity] if joint else (first_rows[g], second_rows)[t]
                            pool.indirect_dma_start(out=rows[parity][:, g * FILL_M + m, half, c0:c1], out_offset=None,
                                                    in_=source[half] if joint else source,
                                                    in_offset=at).then_inc(arrived, 16)

            def gather_w1(t):
                for Q in range(QUARTERS):
                    for n in range(t * FILL_M, (t + 1) * FILL_M):
                        at = bass.IndirectOffsetOnAxis(ap=idx[:, Q * NM + n:Q * NM + n + 1], axis=0)
                        pool.indirect_dma_start(out=w1_all[:, Q, n:n + 1], out_offset=None, in_=w1,
                                                in_offset=at).then_inc(w1_first, 16)

            def refill(t, parity, w1_free):
                pool.wait_ge(rows_turned, 2 * (t - 1))
                if w1_free:
                    pool.wait_ge(w1_kept, 2 * (t - 3))
                gather(t, parity, table)

            pool.wait_ge(idx_ready, 1)
            gather(0, 0, emb_v)
            pool.wait_ge(idx_ready, 2)
            gather(1, 1, emb_v)
            pool.wait_ge(table_stored, 64)
            refill(2, 0, False)
            gather_w1(0)
            refill(3, 1, False)
            gather_w1(1)
            with pool.Fori(4, FILLS - 1, 2) as t:
                refill(t, 0, True)
                refill(t + 1, 1, True)

        @block.vector
        def _(dve):
            dve.wait_ge(idx_loaded, 16 * QUARTERS)
            for k, (m0, m1) in enumerate(((0, FILL_M), (FILL_M, NM))):
                raws, wrap, total, ok = [z[:, :].rearrange("p (a m) -> p a m", a=QUARTERS)[:, :, m0:m1]
                                         for z in (idx_raw, idx_wrap, idx_sum, idx)]
                nc.vector.tensor_scalar(wrap, raws, 0.0, float(VOCAB), ALU.is_lt, ALU.mult).then_inc(idx_chain, 1)
                dve.wait_ge(idx_chain, 2 * k + 1)
                nc.vector.tensor_tensor(total, raws, wrap, ALU.add).then_inc(idx_chain, 1)
                dve.wait_ge(idx_chain, 2 * k + 2)
                nc.vector.tensor_scalar(ok, total, 0.0, float(VOCAB - 1), ALU.max, ALU.min).then_inc(idx_ready, 1)

            nc.vector.memset(zeros[:, :], 0.0)
            nc.vector.memset(score_w[:, :, :], 0.0).then_inc(score_w_cleared, 1)
            nc.vector.memset(pick[:, :, :], 0.0).then_inc(mask_chain, 1)
            dve.wait_ge(iotas_ready, 1)
            dve.wait_ge(mask_chain, 1)
            for Q in range(QUARTERS):
                nc.vector.memset(pick[32 * Q:32 * Q + 32, Q, QUARTERS - 1:QUARTERS], 1.0)
            nc.vector.tensor_scalar(imod[:, :], prow_i[:, :], FIELDS - 1, None, ALU.bitwise_and).then_inc(mask_chain, 1)
            dve.wait_ge(mask_chain, 2)
            nc.vector.tensor_copy(irow[:, :], imod[:, :]).then_inc(mask_chain, 1)
            dve.wait_ge(mask_chain, 3)
            nc.vector.tensor_scalar(upper[:, :], jrow_i[:, :], irow[:, :], None, ALU.is_gt).then_inc(mask_chain, 1)
            dve.wait_ge(small_loaded, 16 * 9)
            dve.wait_ge(score_w_cleared, 1)
            for par in range(2):
                rng = slice(64 * par, 64 * par + 64)
                for slot in range(FIELDS // 2):
                    last = nc.vector.tensor_copy(score_w[rng, slot, 2 * slot + par:2 * slot + par + 1], hcol[rng, :])
            last.then_inc(consts_ready, 1)
            dve.wait_ge(mask_chain, 4)

            def pair_sums(t, r):
                if r == 4:
                    dve.wait_ge(gram_ready, t + 1)
                    nc.vector.tensor_tensor(gram[:, :, :], G[:, :, :],
                                            upper[:, :].unsqueeze(1).to_broadcast([128, GROUP, FIELDS]),
                                            ALU.mult).then_inc(gram_masked, 1)
                if r == 5:
                    dve.wait_ge(gram_masked, t + 1)
                    dve.wait_ge(scored, BATCHES * (t + 1))
                    nc.vector.tensor_tensor(prod[:, :, :], S[:, :, :], gram[:, :, :], ALU.mult).then_inc(prod_ready, 1)
                if r == 6:
                    dve.wait_ge(prod_ready, t + 1)
                    nc.vector.tensor_reduce(part[:, bass.ds(t * GROUP, GROUP)], prod[:, :, :], AX.X, ALU.add
                                            ).then_inc(part_ready, 1)

            def join(half, r0, r1):
                dve.wait_ge(raw_loaded, 32)
                e0 = EMB_AT[half]
                nc.vector.tensor_copy(joined[half][:, r0:r1, W1_AT[half]], raw_w1[:, r0:r1]).then_inc(rows_joined, 1)
                nc.vector.tensor_copy(joined[half][:, r0:r1, e0:e0 + EMB], raw[:, r0:r1, :]).then_inc(rows_joined, 1)

            mid, even = TAB_ROWS // 2, TAB_ROWS // 2 * 2
            joins = {7: [(0, 0, mid)], 9: [(0, mid, even), (0, even, TAB_ROWS)],
                     11: [(1, 0, mid)], 13: [(1, mid, even), (1, even, TAB_ROWS)]}

            def products(t, parity, first, last):
                for r, (s, g) in enumerate(ORDER):
                    n = ROUNDS * t + r
                    if r in (0, 4):
                        dve.wait_ge(v_ready, 2 * t + g + 1)
                    if not first or r >= X_SLOTS:
                        dve.wait_ge(z_ready, n + 1 - X_SLOTS)
                    for slot, j0, nj, c0 in segments(s):
                        shape = [128, 2, GROUP, nj]
                        vj = V[parity][:, g, :, j0:FIELDS].unsqueeze(1).to_broadcast(shape)
                        vi = V[parity][:, g, :, 2 * slot:2 * slot + 2].rearrange("p b c -> p c b")
                        xo = X[:, r % X_SLOTS, :, c0:c0 + GROUP * nj].rearrange("p c (b j) -> p c b j", j=nj)
                        last_one = nc.vector.tensor_tensor(xo, vj, vi.unsqueeze(3).to_broadcast(shape), ALU.mult)
                    last_one.then_inc(x_ready, 1)
                    if not first:
                        pair_sums(t - 1, r)
                    if first and r in joins:
                        for part_of_table in joins[r]:
                            join(*part_of_table)

            over_fills(dve, products)
            for r in (4, 5, 6):
                pair_sums(FILLS - 1, r)

        @block.scalar
        def _(act):
            def keep_v(t, parity, first, g):
                act.wait_ge(rows_turned, 2 * t + g + 1)
                if g == 0 and not first:
                    act.wait_ge(x_ready, ROUNDS * (t - 1))
                    act.wait_ge(gram_ready, t - 1)
                nc.scalar.copy(V[parity][:, g, :, :], TR[:, g, :].rearrange("p (b f) -> p b f", f=FIELDS)
                               ).then_inc(v_ready, 1)

            def keep_pv(parity, g):
                nc.scalar.activation(pV[parity][:, g, :, :], TR[:, g, :].rearrange("p (b f) -> p b f", f=FIELDS),
                                     ACT.Copy, scale=pcol[:, 0:1]).then_inc(pv_ready, 1)

            def keep_w1(t, parity):
                flat = rows[parity][:, :, :, :].rearrange("p t h k -> p t (h k)")
                for half in range(2):
                    src = flat[:, :, half * (2 * ROW - 1)].rearrange("p (g m) -> p g m", g=2)
                    nc.scalar.copy(w1_all[:, 2 * half:2 * half + 2, bass.ds(t * FILL_M, FILL_M)], src
                                   ).then_inc(w1_kept, 1)

            act.wait_ge(small_loaded, 16 * 9)
            nc.scalar.activation(warm[:, :], w0_sb[:, :], ACT.Sigmoid).then_inc(sigmoid_loaded, 1)
            keep_v(0, 0, True, 0)
            keep_pv(0, 0)

            def relus(t, parity, first, last):
                for r, (s, g) in enumerate(ORDER):
                    n = ROUNDS * t + r
                    if first and r == 3:
                        keep_v(0, 0, True, 1)
                        keep_pv(0, 1)
                    act.wait_ge(z_ready, n + 1)
                    if r >= H_SLOTS:
                        act.wait_ge(scored, BATCHES * t + (1 if s % 4 < 2 else 2))
                    elif not first:
                        act.wait_ge(scored, BATCHES * t + (-1 if s % 4 < 2 else 0))
                    nc.scalar.activation(H[:, r % H_SLOTS, :, :], Z[:, r % Z_SLOTS, :, :], ACT.Relu,
                                         bias=bias[:, 0:1]).then_inc(hid_ready, 1)
                    if not last:
                        if r == 8:
                            keep_v(t + 1, 1 - parity, first, 0)
                            keep_v(t + 1, 1 - parity, first, 1)
                        if r == 14:
                            keep_pv(1 - parity, 0)
                            keep_pv(1 - parity, 1)
                        if r == 15 and not first:
                            keep_w1(t + 1, 1 - parity)

            over_fills(act, relus)
            act.wait_ge(logit_ready, 1)
            nc.scalar.activation(y_sb[:, :, :].rearrange("a q m -> a m q"), logit.rearrange("a (m q) -> a m q", q=QUARTERS),
                                 ACT.Sigmoid, bias=w0_sb[:, 0:1]).then_inc(y_ready, 1)

        @block.tensor
        def _(pe):
            def turn(t, parity, groups=(0, 1)):
                embs = rows[parity][:, :, :, :].rearrange("p t h k -> p t (h k)")
                if isinstance(t, int) and t == 0:
                    pe.wait_ge(first_rows[groups[0]], 16 * GATHERS // 2)
                elif isinstance(t, int) and t == 1:
                    pe.wait_ge(second_rows, 16 * GATHERS)
                else:
                    pe.wait_ge(rows_gathered[parity], gathered(t, parity))
                for g in groups:
                    for m in range(FILL_M):
                        last = nc.tensor.transpose(TR[:, g, 128 * m:128 * m + 128],
                                                   embs[:, g * FILL_M + m, 1:1 + 2 * EMB], ident[:, :])
                    last.then_inc(rows_turned, 1)

            def keep_busy(n):
                for _ in range(n):
                    nc.tensor.matmul(S[0:32, :, :], zeros[:, 0:32], zeros[:, :].rearrange("p (b j) -> p b j", j=FIELDS),
                                     start=True, stop=True)

            def hidden(t, r, first):
                n = ROUNDS * t + r
                pe.wait_ge(x_ready, n + 1)
                if not first or r >= Z_SLOTS:
                    pe.wait_ge(hid_ready, n + 1 - Z_SLOTS)
                pe.nop(nofuse=True)
                for half, par in ((0, 0), (0, 1), (1, 0), (1, 1)):
                    k, c = 64 * half, 64 * par
                    last = nc.tensor.matmul(Z[c:c + 64, r % Z_SLOTS, half, :], w_sb[k:k + 64, :],
                                            X[k:k + 64, r % X_SLOTS, par, :], start=True, stop=True)
                last.then_inc(z_ready, 1)

            def clear_scores(t, first):
                if not first:
                    pe.wait_ge(prod_ready, t)
                for Q in range(QUARTERS):
                    nc.tensor.matmul(S[32 * Q:32 * Q + 32, :, :], zeros[:, 0:32],
                                     zeros[:, :].rearrange("p (b j) -> p b j", j=FIELDS), start=True, stop=False)

            def scores(t, steps):
                r_last = ORDER.index((steps[-1], 1))
                pe.wait_ge(hid_ready, ROUNDS * t + r_last + 1)
                for s, (slot, j0, nj, c0) in [(s, piece) for s in steps for piece in segments(s)]:
                    for g in range(2):
                        for half in range(2):
                            Q = 2 * half + g
                            hid = H[:, ORDER.index((s, g)) % H_SLOTS, half, c0:c0 + GROUP * nj]
                            last = nc.tensor.matmul(S[32 * Q:32 * Q + 32, :, j0:FIELDS],
                                                    score_w[:, slot, :],
                                                    hid.rearrange("p (b j) -> p b j", j=nj),
                                                    start=False, stop=(s == STEPS - 1 and c0 > 0))
                last.then_inc(scored, 1)

            def grams(t, parity, first, r):
                if r == min(GRAMS_AFTER):
                    pe.wait_ge(pv_ready, 2 * t + 2)
                    if not first:
                        pe.wait_ge(gram_masked, t)
                    pe.nop(nofuse=True)
                at = GRAMS_AFTER.index(r) * GROUP // len(GRAMS_AFTER)
                for b in range(at, at + GROUP // len(GRAMS_AFTER)):
                    for Q in range(QUARTERS):
                        half, g = divmod(Q, 2)
                        k = slice(64 * half, 64 * half + 64)
                        last = nc.tensor.matmul(G[32 * Q:32 * Q + 32, b, :], V[parity][k, g, b, :],
                                                pV[parity][k, g, b, :], start=(b == 0), stop=(b == GROUP - 1),
                                                skip_group_check=True)
                if r == max(GRAMS_AFTER):
                    last.then_inc(gram_ready, 1)

            pe.wait_ge(ident_ready, 1)
            pe.wait_ge(consts_ready, 1)
            turn(0, 0, (0,))
            keep_busy(8)

            def products(t, parity, first, last):
                for r in range(ROUNDS):
                    hidden(t, r, first)
                    if first and r == 3:
                        turn(0, 0, (1,))
                        keep_busy(8)
                    if r == 8 and not last:
                        pe.wait_ge(pv_ready, 2 * t + 2)
                        turn(t + 1, 1 - parity)
                    if r in SCORED_AFTER:
                        if r == min(SCORED_AFTER):
                            clear_scores(t, first)
                        scores(t, SCORED_AFTER[r])
                    if r == 10 and last:
                        linear_term()
                    if r == LAST_AFTER and not first:
                        scores(t - 1, LAST_STEPS)
                    if r in GRAMS_AFTER:
                        grams(t, parity, first, r)

            def linear_term():
                pe.wait_ge(pv_ready, 2 * FILLS)
                pe.wait_ge(w1_first, 2 * 16 * GATHERS)
                pe.wait_ge(w1_kept, 2 * (FILLS - 2))
                by_q = logit.rearrange("a (m q) -> a q m", q=QUARTERS)
                for q in range(QUARTERS):
                    for Q in range(QUARTERS):
                        nc.tensor.matmul(by_q[:, q, :], pick[:, q, QUARTERS - 1 - Q:2 * QUARTERS - 1 - Q],
                                         w1_all[:, Q, :], start=(q == 0 and Q == 0), stop=False,
                                         skip_group_check=True)

            over_fills(pe, products)
            scores(FILLS - 1, LAST_STEPS)

            for done, c0, c1 in ((FILLS - 1, 0, GROUP * (FILLS - 1)), (FILLS, GROUP * (FILLS - 1), GROUP * FILLS)):
                pe.wait_ge(part_ready, done)
                last = nc.tensor.matmul(logit[:, c0:c1], pick[:, :, QUARTERS - 1], part[:, c0:c1],
                                        start=False, stop=True, skip_group_check=True)
            last.then_inc(logit_ready, 1)


_INS = ["r_x", "L0_rec_emb_v", "L0_rec_at_w", "L0_rec_at_b", "L0_rec_at_h", "L0_rec_p", "L0_rec_w0", "L0_rec_w1"]


def kernel(**inputs):
    import numpy as _np
    import concourse.bacc as _bacc
    from concourse import mybir as _mybir
    from concourse.bass_utils import run_bass_kernel_spmd as _run

    nc = _bacc.Bacc("TRN2", target_bir_lowering=False, num_devices=1)
    arrays, args = {}, []
    for name in _INS:
        a = _np.ascontiguousarray(inputs[name])
        if a.ndim == 0:
            a = a.reshape(1, 1)
        arrays[f"in_{name}_dram"] = a
        args.append(nc.dram_tensor(f"in_{name}_dram", a.shape, _mybir.dt.from_np(a.dtype), kind="ExternalInput").ap())
    out = nc.dram_tensor("out_dram", (BATCH, 1), _mybir.dt.float32, kind="ExternalOutput").ap()
    afm_kernel(nc, *args, out)
    r = _run(nc, [arrays], core_ids=[0])
    return r.results[0]["out_dram"]
```

```python
from contextlib import ExitStack

import concourse.bass as bass
from concourse import mybir

FIELDS, BATCH, EMB, HID, VOCAB = 32, 2048, 64, 64, 12500
QUARTERS = 4
NB = BATCH // QUARTERS
NM = NB // QUARTERS
FILL_M = 4
FILLS = NM // FILL_M
GROUP = FILL_M * QUARTERS
TILES = 2 * FILL_M
GATHERS = 2 * TILES
STEPS = FIELDS // 4
ROUNDS = 2 * STEPS
COLS = GROUP * FIELDS
ORDER = [(s, g) for four in (0, 4) for g in range(2) for s in range(four, four + 4)]
SCORED_AFTER = {7: (0, 1), 9: (2, 3), 15: (4, 5)}
LAST_STEPS, LAST_AFTER = (6, 7), 1
GRAMS_AFTER = (3, 5, 11, 13)
SPLIT = tuple(r for r in range(ROUNDS) if r % 8 in (0, 1, 3, 5, 7))
SPLIT_FROM = 10
LOWER_BEHIND = 2
COPY_AHEAD = 3
BATCHES = 4
X_SLOTS, Z_SLOTS, H_SLOTS, SPLIT_SLOTS = 8, 2, 8, 5
ROW = EMB + 1
EMB_AT, W1_AT = (1, 0), (0, EMB)
TAB_ROWS = VOCAB // 128
TAB_TAIL = VOCAB - 128 * TAB_ROWS
JOINS = ((0, 48), (48, 96), (96, TAB_ROWS))
STORES = tuple((r, r + 12 if r < 84 else TAB_ROWS) for r in range(0, 96, 12))


def segments(s):
    n = FIELDS - 1 - 2 * s
    return [(s, FIELDS - n, n, 0), (STEPS * 2 - 1 - s, n, FIELDS - n, GROUP * n)]


def afm_kernel(nc, r_x, emb_v, at_w, at_b, at_h, p, w0, w1, out):
    fp32, fp32r, bf16 = mybir.dt.float32, mybir.dt.float32r, mybir.dt.bfloat16
    int32, uint32 = mybir.dt.int32, mybir.dt.uint32
    ALU = mybir.AluOpType
    ACT = mybir.ActivationFunctionType
    AX = mybir.AxisListType

    table = [nc.dram_tensor(f"table{half}", (VOCAB, ROW), fp32, kind="Internal").ap() for half in range(2)]

    ctx = ExitStack()
    with ctx:
        def sb(name, shape, dt=fp32):
            return ctx.enter_context(nc.sbuf_tensor(name, shape, dt))

        def ps(name, shape):
            return ctx.enter_context(nc.psum_tensor(name, shape, fp32))

        def sem(name):
            return ctx.enter_context(nc.semaphore(name))

        w_sb = sb("w_sb", [128, 2 * HID])
        w_hi = sb("w_hi", [128, 2 * HID], fp32r)
        w_lo = sb("w_lo", [128, 2 * HID], fp32r)
        bias = sb("bias", [128, 1])
        hcol = sb("hcol", [128, 1])
        pcol = sb("pcol", [128, 1])
        w0_sb = sb("w0_sb", [QUARTERS, 1])
        ident = sb("ident", [128, 128])
        score_w = sb("score_w", [128, FIELDS // 2, FIELDS])
        zeros = sb("zeros", [128, COLS], bf16)
        upper = sb("upper", [128, FIELDS])
        jrow_i = sb("jrow_i", [128, FIELDS], int32)
        prow_i = sb("prow_i", [128, 1], int32)
        bits_i = sb("bits_i", [128, 4], int32)
        row_i = sb("row_i", [128, 1])
        row_q = sb("row_q", [128, 1])
        pick_Q = sb("pick_Q", [128, QUARTERS])
        pick = sb("pick", [128, QUARTERS, 2 * QUARTERS - 1])
        idx_raw = sb("idx_raw", [128, NB], int32)
        idx = sb("idx", [128, NB], uint32)
        idx_stage = [sb(f"idx_stage{i}", [128, QUARTERS, FILL_M], uint32) for i in range(2)]
        raw = sb("raw", [128, TAB_ROWS, EMB])
        raw_w1 = sb("raw_w1", [128, TAB_ROWS])
        joined = sb("joined", [128, TAB_ROWS + 1, ROW + 1])
        rows = [sb(f"rows{i}", [128, TILES, 2, ROW]) for i in range(2)]
        V = [sb(f"V{i}", [128, 2, GROUP, FIELDS]) for i in range(2)]
        pV = [sb(f"pV{i}", [128, 2, GROUP, 2, 2, FIELDS // 2]) for i in range(2)]
        X = sb("X", [128, X_SLOTS, 2, COLS])
        X_split = sb("X_split", [128, 2, SPLIT_SLOTS, 2, COLS], fp32r)
        X_hi, X_lo = X_split[:, 0, :, :, :], X_split[:, 1, :, :, :]
        H = sb("H", [128, H_SLOTS, 2, COLS])
        gram = sb("gram", [128, GROUP, FIELDS])
        prod = sb("prod", [128, GROUP, FIELDS])
        idx_wrap, idx_sum = [z[:, :, :].rearrange("p b j -> p (b j)") for z in (gram, prod)]
        part = sb("part", [128, FILLS * GROUP])
        w1_all = sb("w1_all", [128, QUARTERS, NM])
        y_sb = sb("y_sb", [QUARTERS, QUARTERS, NM])
        warm = sb("warm", [QUARTERS, 1])

        Z = ps("Z", [128, Z_SLOTS, 2, COLS])
        S = ps("S", [128, GROUP, FIELDS])
        G = ps("G", [128, GROUP, FIELDS])
        TR = ps("TR", [128, 2, COLS])
        logit = TR[0:QUARTERS, 0, :]

        idx_loaded = sem("idx_loaded")
        idx_chain = sem("idx_chain")
        idx_ready = sem("idx_ready")
        idx_staged = sem("idx_staged")
        raw_loaded = sem("raw_loaded")
        tail_loaded = sem("tail_loaded")
        rows_joined = sem("rows_joined")
        third_w1 = sem("third_w1")
        table_stored = [sem(f"table_stored{half}") for half in range(2)]
        small_loaded = sem("small_loaded")
        iotas_ready = sem("iotas_ready")
        mask_chain = sem("mask_chain")
        consts_ready = sem("consts_ready")
        w_diag_cleared = sem("w_diag_cleared")
        pv_cleared = sem("pv_cleared")
        w_split = sem("w_split")
        score_w_cleared = sem("score_w_cleared")
        ident_cleared = sem("ident_cleared")
        ident_ready = sem("ident_ready")
        w1_first = sem("w1_first")
        first_rows = [sem(f"first_rows{g}") for g in range(2)]
        second_rows = sem("second_rows")
        rows_gathered = [sem(f"rows_gathered{i}") for i in range(2)]
        rows_turned = sem("rows_turned")
        w1_kept = sem("w1_kept")
        v_ready = sem("v_ready")
        pv_ready = sem("pv_ready")
        x_ready = sem("x_ready")
        x_hi_ready = sem("x_hi_ready")
        x_lo_ready = sem("x_lo_ready")
        z_ready = sem("z_ready")
        hid_ready = sem("hid_ready")
        scored = sem("scored")
        gram_ready = sem("gram_ready")
        gram_masked = sem("gram_masked")
        prod_ready = sem("prod_ready")
        part_ready = sem("part_ready")
        sigmoid_loaded = sem("sigmoid_loaded")
        logit_ready = sem("logit_ready")
        y_ready = sem("y_ready")
        y_stored = sem("y_stored")

        block = ctx.enter_context(nc.Block())

        def over_fills(eng, fill):
            fill(0, 0, True, False)
            with eng.Fori(1, FILLS - 2, 2) as t:
                fill(t, 1, False, False)
                fill(t + 1, 0, False, False)
            fill(FILLS - 1, (FILLS - 1) % 2, False, True)

        def gathered(t, parity):
            return 16 * GATHERS // 2 * (t - parity)

        def is_split(r, first):
            return r in SPLIT and (not first or r >= SPLIT_FROM)

        def split_count(t, r):
            return len(SPLIT) * t + len([z for z in SPLIT if z <= r]) - len([z for z in SPLIT if z < SPLIT_FROM])

        @block.sync
        def _(sp):
            for q in range(QUARTERS):
                sp.dma_start(idx_raw[q * FIELDS:(q + 1) * FIELDS, :],
                             r_x[:, q * NB:(q + 1) * NB]).then_inc(idx_loaded, 16)
            for half in range(2):
                lo, hi = half * 64, half * 64 + 64
                sp.dma_start(pcol[lo:hi, :], p).then_inc(small_loaded, 16)
                sp.dma_start(bias[lo:hi, :], at_b.rearrange("(h o) -> h o", o=1)).then_inc(small_loaded, 16)
                sp.dma_start(hcol[lo:hi, :], at_h).then_inc(small_loaded, 16)
            sp.dma_start(w0_sb[:, :], w0.to_broadcast([QUARTERS, 1])).then_inc(small_loaded, 16)
            sp.wait_ge(w_diag_cleared, 1)
            for half in range(2):
                sp.dma_start(w_sb[64 * half:64 * half + 64, 64 * half:64 * half + 64], at_w).then_inc(small_loaded, 16)
            sp.wait_ge(first_rows[1], 16 * GATHERS // 2)
            main = 128 * TAB_ROWS
            sp.dma_start(raw[:, :, :], emb_v[0:main, :].rearrange("(p r) k -> p r k", p=128)).then_inc(raw_loaded, 16)
            sp.dma_start(raw_w1[:, :], w1[0:main, :].rearrange("(p r) o -> p (r o)", p=128)).then_inc(raw_loaded, 16)
            tail = joined[0:TAB_TAIL, TAB_ROWS, :]
            sp.dma_start(tail[:, 1:1 + EMB], emb_v[main:VOCAB, :]).then_inc(tail_loaded, 16)
            for c in (0, 1 + EMB):
                sp.dma_start(tail[:, c:c + 1], w1[main:VOCAB, :]).then_inc(tail_loaded, 16)
            sp.wait_ge(tail_loaded, 48)
            for half in range(2):
                sp.dma_start(table[half][main:VOCAB, :], tail[:, half:half + ROW]).then_inc(table_stored[half], 16)
            for k, (r0, r1) in enumerate(STORES):
                sp.wait_ge(rows_joined, 3 * next(j + 1 for j, rows_in in enumerate(JOINS) if rows_in[1] >= r1))
                for half in range(2):
                    sp.wait_ge(table_stored[half], 16 * (k + 1))
                    sp.dma_start(table[half][0:main, :].rearrange("(p r) k -> p r k", p=128)[:, r0:r1, :],
                                 joined[:, r0:r1, half:half + ROW]).then_inc(table_stored[half], 16)
            sp.wait_ge(y_ready, 1)
            sp.dma_start(out.rearrange("(q a m) o -> a q (m o)", q=QUARTERS, a=QUARTERS), y_sb[:, :, :]).then_inc(y_stored, 16)
            sp.wait_ge(y_stored, 16)

        @block.gpsimd
        def _(pool):
            nc.gpsimd.iota(prow_i[:, :], pattern=[[0, 1]], base=0, channel_multiplier=1)
            nc.gpsimd.iota(jrow_i[:, :], pattern=[[1, FIELDS]], base=0, channel_multiplier=0).then_inc(iotas_ready, 1)
            nc.gpsimd.memset(ident[:, :], 0.0).then_inc(ident_cleared, 1)
            pool.wait_ge(ident_cleared, 1)
            nc.gpsimd.affine_select(out=ident[:, :], in_=ident[:, :], compare_op=ALU.not_equal, fill=1.0, base=0,
                                    pattern=[[-1, 128]], channel_multiplier=1).then_inc(ident_ready, 1)

            def gather(t, parity, source):
                stage = idx_stage[parity]
                nc.gpsimd.tensor_copy(stage[:, :, :],
                                      idx[:, :].rearrange("p (a m) -> p a m", a=QUARTERS)[:, :, bass.ds(t * FILL_M, FILL_M)]
                                      ).then_inc(idx_staged, 1)
                pool.wait_ge(idx_staged, t + 1)
                pool.nop(nofuse=True)
                for g in range(2):
                    for m in range(FILL_M):
                        for half in range(2):
                            at = bass.IndirectOffsetOnAxis(ap=stage[:, 2 * half + g, m:m + 1], axis=0)
                            joint = source is table
                            c0, c1 = (0, ROW) if joint else (EMB_AT[half], EMB_AT[half] + EMB)
                            arrived = rows_gathered[parity] if joint or t == 2 else (first_rows[g], second_rows)[t]
                            pool.indirect_dma_start(out=rows[parity][:, g * FILL_M + m, half, c0:c1], out_offset=None,
                                                    in_=source[half] if joint else source,
                                                    in_offset=at).then_inc(arrived, 16)

            def gather_third_w1():
                for g in range(2):
                    for m in range(FILL_M):
                        for half in range(2):
                            at = bass.IndirectOffsetOnAxis(ap=idx_stage[0][:, 2 * half + g, m:m + 1], axis=0)
                            c = W1_AT[half]
                            pool.indirect_dma_start(out=rows[0][:, g * FILL_M + m, half, c:c + 1], out_offset=None,
                                                    in_=w1, in_offset=at).then_inc(third_w1, 16)

            def gather_w1(t):
                for Q in range(QUARTERS):
                    for n in range(t * FILL_M, (t + 1) * FILL_M):
                        at = bass.IndirectOffsetOnAxis(ap=idx[:, Q * NM + n:Q * NM + n + 1], axis=0)
                        pool.indirect_dma_start(out=w1_all[:, Q, n:n + 1], out_offset=None, in_=w1,
                                                in_offset=at).then_inc(w1_first, 16)

            def refill(t, parity):
                pool.wait_ge(rows_turned, 2 * (t - 1))
                pool.wait_ge(w1_kept, 2 * (t - 3))
                gather(t, parity, table)

            pool.wait_ge(idx_ready, 1)
            gather(0, 0, emb_v)
            pool.wait_ge(idx_ready, 2)
            gather(1, 1, emb_v)
            pool.wait_ge(rows_turned, 2)
            gather(2, 0, emb_v)
            gather_third_w1()
            for half in range(2):
                pool.wait_ge(table_stored[half], 16 * (1 + len(STORES)))
            pool.wait_ge(rows_turned, 4)
            gather(3, 1, table)
            with pool.Fori(4, FILLS - 1, 2) as t:
                refill(t, 0)
                refill(t + 1, 1)
            gather_w1(0)
            gather_w1(1)

        @block.vector
        def _(dve):
            dve.wait_ge(idx_loaded, 16 * QUARTERS)
            for k, (m0, m1) in enumerate(((0, FILL_M), (FILL_M, NM))):
                raws, wrap, total, ok = [z[:, :].rearrange("p (a m) -> p a m", a=QUARTERS)[:, :, m0:m1]
                                         for z in (idx_raw, idx_wrap, idx_sum, idx)]
                nc.vector.tensor_scalar(wrap, raws, 0.0, float(VOCAB), ALU.is_lt, ALU.mult).then_inc(idx_chain, 1)
                dve.wait_ge(idx_chain, 2 * k + 1)
                nc.vector.tensor_tensor(total, raws, wrap, ALU.add).then_inc(idx_chain, 1)
                dve.wait_ge(idx_chain, 2 * k + 2)
                nc.vector.tensor_scalar(ok, total, 0.0, float(VOCAB - 1), ALU.max, ALU.min).then_inc(idx_ready, 1)

            nc.vector.memset(w_sb[:, :], 0.0).then_inc(w_diag_cleared, 1)
            nc.vector.memset(zeros[:, :], 0.0)
            nc.vector.memset(score_w[:, :, :], 0.0).then_inc(score_w_cleared, 1)
            nc.vector.memset(pick[:, :, :], 0.0).then_inc(mask_chain, 1)
            dve.wait_ge(iotas_ready, 1)
            dve.wait_ge(mask_chain, 1)
            for Q in range(QUARTERS):
                nc.vector.memset(pick[32 * Q:32 * Q + 32, Q, QUARTERS - 1:QUARTERS], 1.0)
            nc.vector.tensor_scalar(bits_i[:, 0:1], prow_i[:, :], 15, 1, ALU.bitwise_and, ALU.logical_shift_left)
            nc.vector.tensor_scalar(bits_i[:, 1:2], prow_i[:, :], 5, 1, ALU.logical_shift_right, ALU.bitwise_and)
            nc.vector.tensor_scalar(bits_i[:, 2:3], prow_i[:, :], 3, 2, ALU.logical_shift_right, ALU.bitwise_and)
            nc.vector.tensor_scalar(bits_i[:, 3:4], prow_i[:, :], 6, None, ALU.logical_shift_right).then_inc(mask_chain, 1)
            dve.wait_ge(mask_chain, 2)
            nc.vector.tensor_tensor(row_i[:, :], bits_i[:, 0:1], bits_i[:, 1:2], ALU.add)
            nc.vector.tensor_tensor(row_q[:, :], bits_i[:, 2:3], bits_i[:, 3:4], ALU.add).then_inc(mask_chain, 1)
            dve.wait_ge(mask_chain, 3)
            nc.vector.tensor_scalar(upper[:, :], jrow_i[:, :], row_i[:, :], None, ALU.is_gt)
            nc.vector.tensor_scalar(pick_Q[:, :], jrow_i[:, 0:QUARTERS], row_q[:, :], None, ALU.is_equal).then_inc(mask_chain, 1)
            dve.wait_ge(small_loaded, 16 * 9)
            dve.wait_ge(score_w_cleared, 1)
            for half in range(2):
                rng = slice(64 * half, 64 * half + 64)
                for slot in range(FIELDS // 2):
                    c = half * (FIELDS // 2) + slot
                    last = nc.vector.tensor_copy(score_w[rng, slot, c:c + 1], hcol[rng, :])
            last.then_inc(consts_ready, 1)
            nc.vector.tensor_copy(w_hi[:, :], w_sb[:, :]).then_inc(w_split, 1)
            dve.wait_ge(w_split, 1)
            nc.vector.tensor_tensor(w_lo[:, :], w_sb[:, :], w_hi[:, :].bitcast(fp32), ALU.subtract).then_inc(w_split, 1)
            for parity in range(2):
                nc.vector.memset(pV[parity][:, :, :, :, :, :], 0.0).then_inc(pv_cleared, 1)
            dve.wait_ge(mask_chain, 4)

            def lower_halves(t, r):
                k = SPLIT.index(r)
                dve.wait_ge(x_hi_ready, split_count(t, r))
                nc.vector.tensor_tensor(X_lo[:, k % SPLIT_SLOTS, :, :], X[:, r % X_SLOTS, :, :],
                                        X_hi[:, k % SPLIT_SLOTS, :, :].bitcast(fp32), ALU.subtract
                                        ).then_inc(x_lo_ready, 1)

            def pair_sums(t, r):
                if r == 4:
                    dve.wait_ge(gram_ready, t + 1)
                    nc.vector.tensor_tensor(gram[:, :, :], G[:, :, :],
                                            upper[:, :].unsqueeze(1).to_broadcast([128, GROUP, FIELDS]),
                                            ALU.mult).then_inc(gram_masked, 1)
                if r == 5:
                    dve.wait_ge(gram_masked, t + 1)
                    dve.wait_ge(scored, BATCHES * (t + 1))
                    nc.vector.tensor_tensor(prod[:, :, :], S[:, :, :], gram[:, :, :], ALU.mult).then_inc(prod_ready, 1)
                if r == 6:
                    dve.wait_ge(prod_ready, t + 1)
                    nc.vector.tensor_reduce(part[:, bass.ds(t * GROUP, GROUP)], prod[:, :, :], AX.X, ALU.add
                                            ).then_inc(part_ready, 1)

            def join(r0, r1):
                dve.wait_ge(raw_loaded, 32)
                for c in (0, 1 + EMB):
                    nc.vector.tensor_copy(joined[:, r0:r1, c], raw_w1[:, r0:r1]).then_inc(rows_joined, 1)
                nc.vector.tensor_copy(joined[:, r0:r1, 1:1 + EMB], raw[:, r0:r1, :]).then_inc(rows_joined, 1)

            joins = {7: JOINS[0:1], 9: JOINS[1:]}

            def products(t, parity, first, last):
                for r, (s, g) in enumerate(ORDER):
                    n = ROUNDS * t + r
                    if r in (0, 4):
                        dve.wait_ge(v_ready, 2 * t + g + 1)
                    if not first or r >= X_SLOTS:
                        dve.wait_ge(z_ready, n + 1 - X_SLOTS)
                    for slot, j0, nj, c0 in segments(s):
                        shape = [128, 2, GROUP, nj]
                        vj = V[parity][:, g, :, j0:FIELDS].unsqueeze(1).to_broadcast(shape)
                        vi = V[parity][:, g, :, 2 * slot:2 * slot + 2].rearrange("p b c -> p c b")
                        xo = X[:, r % X_SLOTS, :, c0:c0 + GROUP * nj].rearrange("p c (b j) -> p c b j", j=nj)
                        last_one = nc.vector.tensor_tensor(xo, vj, vi.unsqueeze(3).to_broadcast(shape), ALU.mult)
                    last_one.then_inc(x_ready, 1)
                    if r >= LOWER_BEHIND and is_split(r - LOWER_BEHIND, first):
                        lower_halves(t, r - LOWER_BEHIND)
                    if r < LOWER_BEHIND and not first and r + ROUNDS - LOWER_BEHIND in SPLIT:
                        lower_halves(t - 1, r + ROUNDS - LOWER_BEHIND)
                    if not first:
                        pair_sums(t - 1, r)
                    if first and r in joins:
                        for part_of_table in joins[r]:
                            join(*part_of_table)

            over_fills(dve, products)
            for r in range(ROUNDS - LOWER_BEHIND, ROUNDS):
                if r in SPLIT:
                    lower_halves(FILLS - 1, r)
            for r in (4, 5, 6):
                pair_sums(FILLS - 1, r)

        @block.scalar
        def _(act):
            def keep_v(t, parity, first, g):
                act.wait_ge(rows_turned, 2 * t + g + 1)
                if g == 0 and not first:
                    act.wait_ge(x_ready, ROUNDS * (t - 1))
                    act.wait_ge(gram_ready, t - 1)
                nc.scalar.copy(V[parity][:, g, :, :], TR[:, g, :].rearrange("p (b f) -> p b f", f=FIELDS)
                               ).then_inc(v_ready, 1)

            def keep_pv(parity, g):
                for half in range(2):
                    k = slice(64 * half, 64 * half + 64)
                    nc.scalar.activation(pV[parity][k, g, :, :, half, :],
                                         TR[k, g, :].rearrange("p (b i c) -> p b c i", c=2, i=FIELDS // 2),
                                         ACT.Copy, scale=pcol[k, 0:1]).then_inc(pv_ready, 1)

            def upper_halves(t, r):
                k = SPLIT.index(r)
                act.wait_ge(x_ready, ROUNDS * t + r + 1)
                if not (isinstance(t, int) and t == 0):
                    held = SPLIT[k - SPLIT_SLOTS]
                    act.wait_ge(z_ready, ROUNDS * (t if held < r else t - 1) + held + 1)
                nc.scalar.copy(X_hi[:, k % SPLIT_SLOTS, :, :], X[:, r % X_SLOTS, :, :]).then_inc(x_hi_ready, 1)

            def keep_w1(t, parity):
                act.wait_ge(third_w1, 16 * GATHERS)
                flat = rows[parity][:, :, :, :].rearrange("p t h k -> p t (h k)")
                for half in range(2):
                    src = flat[:, :, half * (2 * ROW - 1)].rearrange("p (g m) -> p g m", g=2)
                    nc.scalar.copy(w1_all[:, 2 * half:2 * half + 2, bass.ds(t * FILL_M, FILL_M)], src
                                   ).then_inc(w1_kept, 1)

            act.wait_ge(small_loaded, 16 * 9)
            nc.scalar.activation(warm[:, :], w0_sb[:, :], ACT.Sigmoid).then_inc(sigmoid_loaded, 1)
            act.wait_ge(pv_cleared, 2)
            keep_v(0, 0, True, 0)
            keep_pv(0, 0)

            def relus(t, parity, first, last):
                for r, (s, g) in enumerate(ORDER):
                    n = ROUNDS * t + r
                    if first and r == 3:
                        keep_v(0, 0, True, 1)
                        keep_pv(0, 1)
                    later = (r + COPY_AHEAD) % ROUNDS
                    if r + COPY_AHEAD < ROUNDS and is_split(later, first):
                        upper_halves(t, later)
                    if r + COPY_AHEAD >= ROUNDS and is_split(later, False) and not last:
                        upper_halves(t + 1, later)
                    act.wait_ge(z_ready, n + 1)
                    if r >= H_SLOTS:
                        act.wait_ge(scored, BATCHES * t + (1 if s % 4 < 2 else 2))
                    elif not first:
                        act.wait_ge(scored, BATCHES * t + (-1 if s % 4 < 2 else 0))
                    nc.scalar.activation(H[:, r % H_SLOTS, :, :], Z[:, r % Z_SLOTS, :, :], ACT.Relu,
                                         bias=bias[:, 0:1]).then_inc(hid_ready, 1)
                    if not last:
                        if r == 8:
                            keep_v(t + 1, 1 - parity, first, 0)
                            keep_v(t + 1, 1 - parity, first, 1)
                        if r == 15:
                            keep_pv(1 - parity, 0)
                            keep_pv(1 - parity, 1)
                        if r == 15 and not first:
                            keep_w1(t + 1, 1 - parity)

            over_fills(act, relus)
            act.wait_ge(logit_ready, 1)
            nc.scalar.activation(y_sb[:, :, :].rearrange("a q m -> a m q"), logit.rearrange("a (m q) -> a m q", q=QUARTERS),
                                 ACT.Sigmoid, bias=w0_sb[:, 0:1]).then_inc(y_ready, 1)

        @block.tensor
        def _(pe):
            def turn(t, parity, groups=(0, 1)):
                embs = rows[parity][:, :, :, :].rearrange("p t h k -> p t (h k)")
                if isinstance(t, int) and t == 0:
                    pe.wait_ge(first_rows[groups[0]], 16 * GATHERS // 2)
                elif isinstance(t, int) and t == 1:
                    pe.wait_ge(second_rows, 16 * GATHERS)
                else:
                    pe.wait_ge(rows_gathered[parity], gathered(t, parity))
                for g in groups:
                    for m in range(FILL_M):
                        last = nc.tensor.transpose(TR[:, g, 128 * m:128 * m + 128],
                                                   embs[:, g * FILL_M + m, 1:1 + 2 * EMB], ident[:, :])
                    last.then_inc(rows_turned, 1)

            def keep_busy(n):
                for _ in range(n):
                    nc.tensor.matmul(S[0:32, :, :], zeros[:, 0:32], zeros[:, :].rearrange("p (b j) -> p b j", j=FIELDS),
                                     start=True, stop=True)

            def hidden(t, r, first):
                n = ROUNDS * t + r
                z, x = Z[:, r % Z_SLOTS, :, :], X[:, r % X_SLOTS, :, :]
                split = is_split(r, first)
                if split:
                    k = SPLIT.index(r)
                    pe.wait_ge(x_lo_ready, split_count(t, r))
                    x_hi, x_lo = X_hi[:, k % SPLIT_SLOTS, :, :], X_lo[:, k % SPLIT_SLOTS, :, :]
                else:
                    pe.wait_ge(x_ready, n + 1)
                if not first or r >= Z_SLOTS:
                    pe.wait_ge(hid_ready, n + 1 - Z_SLOTS)
                for par in range(2):
                    if split:
                        nc.tensor.matmul(z[:, par, :], w_hi[:, :], x_hi[:, par, :], start=True, stop=False)
                        nc.tensor.matmul(z[:, par, :], w_hi[:, :], x_lo[:, par, :], start=False, stop=False)
                        last = nc.tensor.matmul(z[:, par, :], w_lo[:, :], x_hi[:, par, :], start=False, stop=True)
                    else:
                        last = nc.tensor.matmul(z[:, par, :], w_sb[:, :], x[:, par, :], start=True, stop=True)
                last.then_inc(z_ready, 1)

            def clear_scores(t, first):
                if not first:
                    pe.wait_ge(prod_ready, t)
                for Q in range(QUARTERS):
                    nc.tensor.matmul(S[32 * Q:32 * Q + 32, :, :], zeros[:, 0:32],
                                     zeros[:, :].rearrange("p (b j) -> p b j", j=FIELDS), start=True, stop=False)

            def scores(t, steps):
                r_last = ORDER.index((steps[-1], 1))
                pe.wait_ge(hid_ready, ROUNDS * t + r_last + 1)
                for s, (slot, j0, nj, c0) in [(s, piece) for s in steps for piece in segments(s)]:
                    for g in range(2):
                        for par in range(2):
                            at = 32 * (2 * g + par)
                            hid = H[:, ORDER.index((s, g)) % H_SLOTS, par, c0:c0 + GROUP * nj]
                            last = nc.tensor.matmul(S[at:at + 32, :, j0:FIELDS],
                                                    score_w[:, slot, :],
                                                    hid.rearrange("p (b j) -> p b j", j=nj),
                                                    start=False, stop=(s == STEPS - 1 and c0 > 0))
                last.then_inc(scored, 1)

            def grams(t, parity, first, r):
                if r == min(GRAMS_AFTER):
                    pe.wait_ge(pv_ready, 4 * t + 4)
                    if not first:
                        pe.wait_ge(gram_masked, t)
                    pe.nop(nofuse=True)
                at = GRAMS_AFTER.index(r) * GROUP // len(GRAMS_AFTER)
                for b in range(at, at + GROUP // len(GRAMS_AFTER)):
                    for g in range(2):
                        for par in range(2):
                            at = 32 * (2 * g + par)
                            last = nc.tensor.matmul(G[at:at + 32, b, :],
                                                    pV[parity][:, g, b, par, :, :].rearrange("p h i -> p (h i)"),
                                                    V[parity][:, g, b, :], start=(b == 0), stop=(b == GROUP - 1),
                                                    skip_group_check=True)
                if r == max(GRAMS_AFTER):
                    last.then_inc(gram_ready, 1)

            pe.wait_ge(ident_ready, 1)
            pe.wait_ge(consts_ready, 1)
            pe.wait_ge(w_split, 2)
            turn(0, 0, (0,))
            keep_busy(8)

            def products(t, parity, first, last):
                for r in range(ROUNDS):
                    hidden(t, r, first)
                    if first and r == 3:
                        turn(0, 0, (1,))
                        keep_busy(8)
                    if r == 8 and not last:
                        pe.wait_ge(pv_ready, 4 * t + 4)
                        turn(t + 1, 1 - parity)
                    if r in SCORED_AFTER:
                        if r == min(SCORED_AFTER):
                            clear_scores(t, first)
                        scores(t, SCORED_AFTER[r])
                    if r == 10 and last:
                        linear_term()
                    if r == LAST_AFTER and not first:
                        scores(t - 1, LAST_STEPS)
                    if r in GRAMS_AFTER:
                        grams(t, parity, first, r)

            def linear_term():
                pe.wait_ge(pv_ready, 4 * FILLS)
                pe.wait_ge(w1_first, 2 * 16 * GATHERS)
                pe.wait_ge(w1_kept, 2 * (FILLS - 2))
                by_q = logit.rearrange("a (m q) -> a q m", q=QUARTERS)
                for q in range(QUARTERS):
                    for Q in range(QUARTERS):
                        nc.tensor.matmul(by_q[:, q, :], pick[:, q, QUARTERS - 1 - Q:2 * QUARTERS - 1 - Q],
                                         w1_all[:, Q, :], start=(q == 0 and Q == 0), stop=False,
                                         skip_group_check=True)

            over_fills(pe, products)
            scores(FILLS - 1, LAST_STEPS)

            for done, c0, c1 in ((FILLS - 1, 0, GROUP * (FILLS - 1)), (FILLS, GROUP * (FILLS - 1), GROUP * FILLS)):
                pe.wait_ge(part_ready, done)
                last = nc.tensor.matmul(logit[:, c0:c1], pick_Q[:, :], part[:, c0:c1],
                                        start=False, stop=True, skip_group_check=True)
            last.then_inc(logit_ready, 1)


_INS = ["r_x", "L0_rec_emb_v", "L0_rec_at_w", "L0_rec_at_b", "L0_rec_at_h", "L0_rec_p", "L0_rec_w0", "L0_rec_w1"]


def kernel(**inputs):
    import numpy as _np
    import concourse.bacc as _bacc
    from concourse import mybir as _mybir
    from concourse.bass_utils import run_bass_kernel_spmd as _run

    nc = _bacc.Bacc("TRN2", target_bir_lowering=False, num_devices=1)
    arrays, args = {}, []
    for name in _INS:
        a = _np.ascontiguousarray(inputs[name])
        if a.ndim == 0:
            a = a.reshape(1, 1)
        arrays[f"in_{name}_dram"] = a
        args.append(nc.dram_tensor(f"in_{name}_dram", a.shape, _mybir.dt.from_np(a.dtype), kind="ExternalInput").ap())
    out = nc.dram_tensor("out_dram", (BATCH, 1), _mybir.dt.float32, kind="ExternalOutput").ap()
    afm_kernel(nc, *args, out)
    r = _run(nc, [arrays], core_ids=[0])
    return r.results[0]["out_dram"]
```
